# Optimizing a Trainium2 kernel written in Bass

```python
import numpy as np
import jax
import jax.numpy as jnp

def _softmax(x, axis=-1):
    return jax.nn.softmax(x, axis=axis)
def _gelu(x):
    return jax.nn.gelu(x, approximate=True)
def _silu(x):
    return jax.nn.silu(x)
def _sigmoid(x):
    return jax.nn.sigmoid(x)
def _layernorm(x, axis=-1, eps=1e-5):
    m = jnp.mean(x, axis=axis, keepdims=True)
    v = jnp.var(x, axis=axis, keepdims=True)
    return (x - m) / jnp.sqrt(v + eps)
def _scatter_add(tgt, idx, src, axis=0):
    return tgt.at[idx].add(src)
def _segment_sum(src, seg, n):
    return jax.ops.segment_sum(src, seg, n)

kernel_name = 'mk_conv_seq_d1_conv_nchw192_8aa788'

def setup_inputs(seed: int = 0):
    np.random.seed(seed)
    _w = jnp.asarray
    def _rec_inputs():
        import jax
        import jax.numpy as jnp
        _gk = jax.random.key(seed)
        x = -0.0001538 + 1 * jax.random.normal(jax.random.fold_in(_gk, 1), (8, 192, 64, 64), jnp.float32)
        return x
    x = _rec_inputs()
    def _L0_conv_setup():
        import jax, jax.numpy as jnp
        import numpy as np
        LATENT = 96
        RDK = LATENT ** 0.5
        key = jax.random.key(seed)
        k1, k2, k3, k4, k5 = jax.random.split(key, 5)
        B, C, H, W = (8, 192, 64, 64)
        x = jax.random.normal(k1, (B, C, H, W), dtype=jnp.float32)
        Wt = jax.random.normal(k2, (3 * LATENT, C), dtype=jnp.float32) * 0.05
        bt = jax.random.normal(k3, (3 * LATENT,), dtype=jnp.float32) * 0.05
        Wd = jax.random.normal(k4, (C, LATENT), dtype=jnp.float32) * 0.05
        bd = jax.random.normal(k5, (C,), dtype=jnp.float32) * 0.05
        return {'x': x, 'Wt': Wt, 'bt': bt, 'Wd': Wd, 'bd': bd}
    _L0_conv_all = _L0_conv_setup()
    _L0_conv_in = {k: v for k, v in _L0_conv_all.items() if k in ('Wt', 'bt', 'Wd', 'bd', )}
    del _L0_conv_all

    return {
        "x": x,
        "L0_conv_Wt": _L0_conv_in["Wt"],
        "L0_conv_bt": _L0_conv_in["bt"],
        "L0_conv_Wd": _L0_conv_in["Wd"],
        "L0_conv_bd": _L0_conv_in["bd"],
    }

def reference(x, L0_conv_Wt, L0_conv_bt, L0_conv_Wd, L0_conv_bd):
    import jax
    import jax.numpy as jnp
    def _L0_conv_ref(x, Wt, bt, Wd, bd):
        import jax, jax.numpy as jnp
        import numpy as np
        LATENT = 96
        RDK = LATENT ** 0.5
        B, C, H, W = x.shape
        N = H * W
        t = jnp.einsum('bchw,oc->bohw', x, Wt) + bt[None, :, None, None]
        Q = t[:, :LATENT]
        V = t[:, LATENT:2 * LATENT]
        K = t[:, 2 * LATENT:]
        Qf = Q.reshape(B, LATENT, N)
        Vf = V.reshape(B, LATENT, N)
        Kf = K.reshape(B, LATENT, N)
        score = jnp.einsum('bcq,bck->bqk', Qf, Kf) / jnp.asarray(RDK, x.dtype)
        index = jax.nn.softmax(score, axis=1)
        out = jnp.einsum('bcq,bqk->bck', Vf, index).reshape(B, LATENT, H, W)
        out = jnp.einsum('bchw,oc->bohw', out, Wd) + bd[None, :, None, None]
        return out + x

    def _gn(v, G=32, eps=1e-5):
        B_, C_, H_, W_ = v.shape
        g = v.reshape(B_, G, C_ // G, H_, W_)
        m = jnp.mean(g, axis=(2, 3, 4), keepdims=True)
        s = jnp.var(g, axis=(2, 3, 4), keepdims=True)
        return ((g - m) / jnp.sqrt(s + eps)).reshape(v.shape)

    def _ln_c(v, eps=1e-6):
        m = jnp.mean(v, axis=1, keepdims=True)
        s = jnp.var(v, axis=1, keepdims=True)
        return (v - m) / jnp.sqrt(s + eps)

    def _ln_t(v, eps=1e-5):
        m = jnp.mean(v, axis=-1, keepdims=True)
        s = jnp.var(v, axis=-1, keepdims=True)
        return (v - m) / jnp.sqrt(s + eps)

    def _to_tokens(v):
        B_, C_, H_, W_ = v.shape
        return v.reshape(B_, C_, H_ * W_).transpose(0, 2, 1)
    def _from_tokens(t, like):
        B_, C_, H_, W_ = like.shape
        return t.transpose(0, 2, 1).reshape(B_, C_, H_, W_)

    x = _L0_conv_ref(x, L0_conv_Wt, L0_conv_bt, L0_conv_Wd, L0_conv_bd)
    return x


_drawn_inputs = setup_inputs


def setup_inputs(seed=0):
    import zlib

    import numpy as np

    out = dict(_drawn_inputs(seed))
    spreads = {}
    factors = {'L0_conv_Wt': 4.226}
    for name, (base, spread) in spreads.items():
        noise = np.random.default_rng([zlib.crc32(name.encode()), seed]).standard_normal(out[name].shape)
        drawn = base * np.exp(spread * noise) if base else spread * noise
        out[name] = jnp.asarray(drawn.astype(out[name].dtype))
    for name, factor in factors.items():
        out[name] = (out[name] * factor).astype(out[name].dtype)
    return out
```

```python
from contextlib import ExitStack

import concourse.bass as bass
from concourse import mybir

F32 = mybir.dt.float32
F32R = mybir.dt.float32r
ALU = mybir.AluOpType
ACT = mybir.ActivationFunctionType
AX = mybir.AxisListType


def attention_conv_kernel(nc, x, wt, bt, wd, out):
    B, C, N = x.shape
    L = wd.shape[0] - 1
    W3 = 3 * L
    P = 128
    R = C - P
    HALVES = 2
    CH = C // HALVES
    CHUNK = 512
    CHUNKS = N // CHUNK
    QT = N // P
    KT = CHUNK // P
    QB = N // CHUNK
    MAXES = KT * QB
    VG = 4
    MADE = 2 * QB + QT // VG
    SCALE = float(L) ** -0.5
    RING = 4
    LAG = 2
    STAGES = 2
    INVERT_SLOT = 6
    SPLIT_SLOT = [4, 26]
    PROJECT_SLOT = [16, 19]

    def max_slot(n):
        return 1 + n * 26 // MAXES

    MAX_IN_SLOT = [[n for n in range(MAXES) if max_slot(n) == t] for t in range(QT)]

    KINDS = [("k", 0)] + [("q", i) for i in range(QB)] + [("k", i) for i in range(1, QB)] \
        + [("v", g) for g in range(QT // VG)]
    READY = 1 + QB
    AFTER = [[] for _ in KINDS]
    for n in range(MAXES):
        AFTER[READY + 1 + n * (MADE - READY - 4) // MAXES].append(n)

    y_view = out.rearrange("b (h c) n -> b c h n", h=HALVES)
    x_view = x.rearrange("b (h c) n -> b c h n", h=HALVES)

    ctx = ExitStack()
    with ctx:
        def sb(name, shape, dt=F32):
            return ctx.enter_context(nc.sbuf_tensor(name, shape, dt))

        def bank(name):
            return ctx.enter_context(nc.psum_tensor(name, [P, CHUNK], F32))

        def sem(name):
            return ctx.enter_context(nc.semaphore(name))

        x_stage = sb("x_stage", [P, STAGES, 2, CHUNK])
        x_hi = sb("x_hi", [P, 2, N], F32R)
        x_lo = sb("x_lo", [P, 2, N], F32R)
        wa_hi = sb("wa_hi", [P, W3], F32R)
        wa_lo = sb("wa_lo", [P, W3], F32R)
        wb_mix = sb("wb_mix", [P, W3], F32R)
        wb_bias = sb("wb_bias", [R + 2, W3], F32R)
        bias_lo = sb("bias_lo", [R + 2, W3], F32R)
        wd_hi = sb("wd_hi", [L + 1, C], F32R)
        wd_lo = sb("wd_lo", [L + 1, C], F32R)
        q_hi = sb("q_hi", [L + 1, N], F32R)
        q_lo = sb("q_lo", [L, N], F32R)
        k_hi = sb("k_hi", [L + 1, N], F32R)
        k_lo = sb("k_lo", [L, N], F32R)
        v_hi = sb("v_hi", [P, QT, L + 2], F32R)
        v_lo = sb("v_lo", [P, QT, L + 2], F32R)
        k_max = sb("k_max", [L, KT, P], F32R)
        part_max = sb("part_max", [P, KT, QB])
        neg_max = sb("neg_max", [P, KT], F32R)
        p_hi = sb("p_hi", [P, RING, CHUNK], F32R)
        p_lo = sb("p_lo", [P, RING, CHUNK], F32R)
        acc_sb = sb("acc_sb", [L + 1, CHUNK])
        sums = sb("sums", [P, KT])
        inverse = sb("inverse", [P, KT])
        inverse_row = sb("inverse_row", [1, CHUNK])
        inverse_all = sb("inverse_all", [P, CHUNK])
        att = sb("att", [L + 1, CHUNK])
        att_hi = sb("att_hi", [L + 1, CHUNK], F32R)
        att_lo = sb("att_lo", [L + 1, CHUNK], F32R)
        x_res = sb("x_res", [CH, HALVES, CHUNK])
        y_sb = sb("y_sb", [CH, HALVES, CHUNK])
        wa_in = x_stage[:, 0, 0, 0:W3]
        wb_in = x_stage[:, 0, 1, 0:W3]
        bias_in = x_stage[R:R + 2, 1, 0, 0:W3]
        wd_in = x_stage[0:L + 1, 1, 1, 0:C]

        s_bank = [bank(f"s_bank{i}") for i in range(RING)]
        m_bank = [bank(f"m_bank{i}") for i in range(2)]
        y_bank = bank("y_bank")
        acc_bank = bank("acc_bank")

        weights_in = sem("weights_in")
        w_hi_done = sem("w_hi_done")
        w_lo_done = sem("w_lo_done")
        bias_moved = sem("bias_moved")
        ones_set = sem("ones_set")
        x_in = [sem(f"x_in{i}") for i in range(STAGES)]
        x_hi_done = sem("x_hi_done")
        x_lo_done = sem("x_lo_done")
        made = sem("made")
        hi_done = sem("hi_done")
        lo_done = sem("lo_done")
        k_copied = sem("k_copied")
        max_made = sem("max_made")
        max_taken = sem("max_taken")
        neg_max_done = sem("neg_max_done")
        max_row_in = sem("max_row_in")
        s_made = sem("s_made")
        p_hi_done = sem("p_hi_done")
        p_done = sem("p_done")
        p_lo_done = sem("p_lo_done")
        pv_done = sem("pv_done")
        acc_out = sem("acc_out")
        sums_in = sem("sums_in")
        inverse_done = sem("inverse_done")
        inverse_row_in = sem("inverse_row_in")
        inverse_spread = sem("inverse_spread")
        att_done = sem("att_done")
        y_made = sem("y_made")
        x_res_in = sem("x_res_in")
        y_done = sem("y_done")
        y_out = sem("y_out")

        def cols(j):
            return bass.ds(j * CHUNK, CHUNK)

        def x_blocks(c):
            return QB + c

        def stage0_loads(blocks):
            return blocks - QB + QB // STAGES

        def walk(eng, make, chunk):
            make(0)
            chunk(0, 0, 0, first=True)
            with eng.Fori(0, B - 1) as b:
                c = b * CHUNKS
                with eng.Fori(1, CHUNKS - 1) as j:
                    chunk(c + j, b, j)
                chunk(c + CHUNKS - 1, b, CHUNKS - 1, last=True)
                make(b + 1)
                chunk(c + CHUNKS, b + 1, 0, first=True)
            c = (B - 1) * CHUNKS
            with eng.Fori(1, CHUNKS - 1) as j:
                chunk(c + j, B - 1, j, final=True)
            chunk(c + CHUNKS - 1, B - 1, CHUNKS - 1, last=True, final=True)

        block = ctx.enter_context(nc.Block())

        @block.sync
        def _(sp):
            def load_x(stage, b, j):
                for dst, c0, c1, part in ((slice(0, R), P, C, 1), (slice(R, P), P, C, 1), (slice(0, P), 0, P, 0)):
                    sp.dma_start(x_stage[dst, stage, part, :], x[b, c0:c1, cols(j)]).then_inc(x_in[stage], 16)

            def y_stored(c):
                sp.wait_ge(y_out, 16 * (c + 1))

            def move_max_row(c, j, stored=None):
                sp.wait_ge(neg_max_done, c + 1)
                if stored is not None:
                    y_stored(stored)
                row = k_hi[L:L + 1, cols(j)].rearrange("o (p t) -> o p t", t=KT)
                sp.dma_start(row.bitcast(F32), neg_max[:, :].bitcast(F32)).then_inc(max_row_in, 16)

            def finish(c, b, j):
                sp.dma_start(x_res[:, :, :], x_view[b, :, :, cols(j)]).then_inc(x_res_in, 16)
                sp.wait_ge(acc_out, c + 1)
                sp.dma_start(sums[:, :], acc_sb[0:1, :].rearrange("o (p t) -> o p t", t=KT)).then_inc(sums_in, 16)
                sp.wait_ge(inverse_done, c + 1)
                sp.dma_start(inverse_row[0:1, :].rearrange("o (p t) -> o p t", t=KT), inverse[:, :])\
                    .then_inc(inverse_row_in, 16)
                sp.wait_ge(inverse_row_in, 16 * (c + 1))
                sp.dma_start(inverse_all[:, :], inverse_row[0:1, None, :].to_broadcast([1, P, CHUNK]))\
                    .then_inc(inverse_spread, 16)
                sp.wait_ge(y_done, HALVES * (c + 1))
                sp.dma_start(y_view[b, :, :, cols(j)], y_sb[:, :, :]).then_inc(y_out, 16)

            def make(b):
                if isinstance(b, int):
                    for j in range(STAGES, QB):
                        sp.wait_ge(x_lo_done, 2 * (j - STAGES + 1))
                        load_x(j % STAGES, 0, j)
                move_max_row(b * CHUNKS, 0)

            def chunk(c, b, j, first=False, last=False, final=False):
                if not first and not final:
                    sp.wait_ge(x_lo_done, 2 * (x_blocks(c) - 1))
                    load_x(0, b + 1, j)
                if first:
                    if not isinstance(c, int):
                        finish(c - 1, b - 1, CHUNKS - 1)
                else:
                    finish(c - 1, b, j - 1)
                if last and not final:
                    sp.wait_ge(x_lo_done, 2 * x_blocks(c))
                    y_stored(c - 1)
                    load_x(0, b + 1, 0)
                elif last:
                    y_stored(c - 1)
                else:
                    move_max_row(c + 1, j + 1, None if isinstance(c, int) and c == 0 else c - 1)

            for src, dst in ((wt[0:P, :], wa_in), (wt[P:C, :], wb_in[0:R, :]), (wt[P:C, :], wb_in[R:P, :]),
                             (bt.to_broadcast([2, W3]), bias_in), (wd, wd_in)):
                sp.dma_start(dst, src).then_inc(weights_in, 16)
            sp.wait_ge(w_lo_done, 4)
            for j in range(STAGES):
                load_x(j, 0, j)
            sp.dma_start(wb_bias[R + 1:R + 2, :].bitcast(F32), bias_lo[R:R + 1, :].bitcast(F32)).then_inc(bias_moved, 16)
            walk(sp, make, chunk)
            finish(B * CHUNKS - 1, B - 1, CHUNKS - 1)
            y_stored(B * CHUNKS - 1)

        @block.gpsimd
        def _(pool):
            def split_x(blocks, j, part, rows, stage=0):
                pool.wait_ge(x_hi_done, blocks)
                nc.gpsimd.tensor_tensor(x_lo[0:rows, part, cols(j)], x_stage[0:rows, stage, part, :],
                                        x_hi[0:rows, part, cols(j)], ALU.subtract).then_inc(x_lo_done, 1)

            def finish(c):
                pool.wait_ge(inverse_spread, 16 * (c + 1))
                for dst in (att, att_hi):
                    nc.gpsimd.tensor_tensor(dst[:, :], acc_sb[:, :], inverse_all[0:L + 1, :], ALU.mult)\
                        .then_inc(att_done, 1)
                pool.wait_ge(att_done, 3 * c + 2)
                nc.gpsimd.tensor_tensor(att_lo[:, :], att[:, :], att_hi[:, :], ALU.subtract).then_inc(att_done, 1)

            def make(b):
                if isinstance(b, int):
                    for j in range(QB):
                        split_x(j + 1, j, 1, R, stage=j % STAGES)

            def chunk(c, b, j, first=False, last=False, final=False):
                if not first and not final:
                    split_x(x_blocks(c), j, 0, P)
                    split_x(x_blocks(c), j, 1, R)
                if not isinstance(c, int) or c > 0:
                    finish(c - 1)
                if last and not final:
                    split_x(x_blocks(c) + 1, 0, 0, P)
                    split_x(x_blocks(c) + 1, 0, 1, R)

            nc.gpsimd.memset(v_hi[:, :, 0:1].bitcast(F32), 1.0).then_inc(ones_set, 1)
            nc.gpsimd.memset(v_lo[:, :, 0:1].bitcast(F32), 0.0).then_inc(ones_set, 1)
            walk(pool, make, chunk)
            finish(B * CHUNKS - 1)

        @block.tensor
        def _(pe):
            def max_products(c, ns):
                for n in ns:
                    if n == 0:
                        pe.wait_ge(k_copied, c + 1)
                    if n >= 2:
                        pe.wait_ge(max_taken, MAXES * c + n - 1)
                    kt, qb = n // QB, n % QB
                    nc.tensor.matmul(m_bank[n % 2][:, :], k_max[:, kt, :], q_hi[0:L, qb * CHUNK:(qb + 1) * CHUNK],
                                     start=True, stop=True).then_inc(max_made, 1)

            def make(b):
                for u, (kind, i) in enumerate(KINDS):
                    if u >= RING:
                        pe.wait_ge(lo_done, MADE * b + u - RING + 1)
                    dst = s_bank[u % RING]
                    if isinstance(b, int) and (kind == "q" or u == 0):
                        pe.wait_ge(x_hi_done, i + 1)
                        pe.wait_ge(x_lo_done, 2 * (i + 1))
                    elif u == 0:
                        pe.wait_ge(x_hi_done, QB * (b + 1))
                        pe.wait_ge(x_lo_done, 2 * QB * (b + 1))
                    if kind == "v":
                        for t in range(VG):
                            q = slice((i * VG + t) * P, (i * VG + t + 1) * P)
                            s = slice(L, 2 * L)
                            o = dst[:, t * L:(t + 1) * L]
                            nc.tensor.matmul(o, x_hi[:, 0, q], wa_hi[:, s], start=True, stop=False)
                            nc.tensor.matmul(o, x_hi[:, 0, q], wa_lo[:, s], start=False, stop=False)
                            nc.tensor.matmul(o, x_lo[:, 0, q], wa_hi[:, s], start=False, stop=False)
                            nc.tensor.matmul(o, x_hi[:, 1, q], wb_mix[:, s], start=False, stop=False)
                            last = nc.tensor.matmul(o, x_lo[0:R + 2, 1, q], wb_bias[:, s], start=False, stop=True)
                    else:
                        s = slice(0, L) if kind == "q" else slice(2 * L, 3 * L)
                        m = slice(i * CHUNK, (i + 1) * CHUNK)
                        o = dst[0:L, :]
                        nc.tensor.matmul(o, wa_hi[:, s], x_hi[:, 0, m], start=True, stop=False)
                        nc.tensor.matmul(o, wa_lo[:, s], x_hi[:, 0, m], start=False, stop=False)
                        nc.tensor.matmul(o, wa_hi[:, s], x_lo[:, 0, m], start=False, stop=False)
                        nc.tensor.matmul(o, wb_mix[:, s], x_hi[:, 1, m], start=False, stop=False)
                        last = nc.tensor.matmul(o, wb_bias[:, s], x_lo[0:R + 2, 1, m], start=False, stop=True)
                    last.then_inc(made, 1)
                    if u == READY:
                        pe.wait_ge(hi_done, MADE * b + READY)
                    max_products(b * CHUNKS, AFTER[u])
                pe.wait_ge(lo_done, MADE * (b + 1))

            def add_pv(c, t):
                pe.wait_ge(p_lo_done, QT * c + t + 1)
                for i, (v, p) in enumerate(((v_hi, p_hi), (v_lo, p_hi), (v_hi, p_lo))):
                    last = nc.tensor.matmul(acc_bank[0:L + 1, :], v[:, t, 0:L + 1], p[:, t % RING, :],
                                            start=(t == 0 and i == 0), stop=(t == QT - 1 and i == 2))
                last.then_inc(pv_done, 1)

            def project(c, h):
                if h == 0:
                    pe.wait_ge(att_done, 3 * (c + 1))
                else:
                    pe.wait_ge(y_done, HALVES * c + h)
                s = slice(h * CH, (h + 1) * CH)
                nc.tensor.matmul(y_bank[0:CH, :], wd_hi[:, s], att_hi[:, :], start=True, stop=False)
                nc.tensor.matmul(y_bank[0:CH, :], wd_lo[:, s], att_hi[:, :], start=False, stop=False)
                nc.tensor.matmul(y_bank[0:CH, :], wd_hi[:, s], att_lo[:, :], start=False, stop=True)\
                    .then_inc(y_made, 1)

            def chunk(c, b, j, first=False, last=False, final=False):
                start = isinstance(c, int) and c == 0
                pe.wait_ge(max_row_in, 16 * (c + 1))
                for t in range(QT):
                    q = slice(t * P, (t + 1) * P)
                    dst = s_bank[t % RING][:, :]
                    nc.tensor.matmul(dst, q_hi[:, q], k_hi[:, cols(j)], start=True, stop=False)
                    nc.tensor.matmul(dst, q_hi[0:L, q], k_lo[:, cols(j)], start=False, stop=False)
                    nc.tensor.matmul(dst, q_lo[:, q], k_hi[0:L, cols(j)], start=False, stop=True).then_inc(s_made, 1)
                    if not last:
                        max_products(c + 1, MAX_IN_SLOT[t])
                    if t in PROJECT_SLOT and not start:
                        project(c - 1, PROJECT_SLOT.index(t))
                    if t >= LAG:
                        if t == LAG and not start:
                            pe.wait_ge(acc_out, c)
                        add_pv(c, t - LAG)
                    elif not first:
                        add_pv(c - 1, t - LAG + QT)
                if last:
                    for t in range(QT - LAG, QT):
                        add_pv(c, t)

            pe.wait_ge(w_lo_done, 4)
            pe.wait_ge(w_hi_done, 4)
            pe.wait_ge(bias_moved, 16)
            pe.wait_ge(ones_set, 4)
            walk(pe, make, chunk)
            for h in range(HALVES):
                project(B * CHUNKS - 1, h)

        @block.scalar
        def _(act):
            def split_x(j, loads, stage=0):
                act.wait_ge(x_in[stage], 48 * loads)
                nc.scalar.activation(x_hi[:, :, cols(j)], x_stage[:, stage, :, :], ACT.Copy).then_inc(x_hi_done, 1)

            def copy_k(c, j):
                src = k_hi[0:L, cols(j)].rearrange("l (p t) -> l t p", t=KT)
                nc.scalar.activation(k_max[:, :, :], src, ACT.Copy).then_inc(k_copied, 1)

            def store_acc(c):
                act.wait_ge(pv_done, QT * (c + 1))
                nc.scalar.activation(acc_sb[:, :], acc_bank[0:L + 1, :], ACT.Copy).then_inc(acc_out, 1)

            def make(b):
                for u, (kind, i) in enumerate(KINDS):
                    if isinstance(b, int) and (kind == "q" or u == 0):
                        if u != 1:
                            split_x(i, i // STAGES + 1, i % STAGES)
                    act.wait_ge(made, MADE * b + u + 1)
                    src = s_bank[u % RING]
                    if kind == "v":
                        nc.scalar.activation(v_hi[:, i * VG:(i + 1) * VG, 1:L + 1],
                                             src[:, 0:VG * L].rearrange("p (t l) -> p t l", t=VG), ACT.Copy)\
                            .then_inc(hi_done, 1)
                    else:
                        dst = q_hi if kind == "q" else k_hi
                        nc.scalar.activation(dst[0:L, i * CHUNK:(i + 1) * CHUNK], src[0:L, :], ACT.Copy)\
                            .then_inc(hi_done, 1)
                    if u == 0:
                        act.wait_ge(hi_done, MADE * b + 1)
                        copy_k(b * CHUNKS, 0)

            def chunk(c, b, j, first=False, last=False, final=False):
                if not last:
                    act.wait_ge(hi_done, MADE * (b + 1))
                    act.wait_ge(max_made, MAXES * (c + 1))
                    copy_k(c + 1, j + 1)
                for t in range(QT):
                    s = s_bank[t % RING][:, :]
                    act.wait_ge(s_made, QT * c + t + 1)
                    if t >= RING or not first:
                        act.wait_ge(pv_done, QT * c + t - RING + 1)
                    nc.scalar.activation(p_hi[:, t % RING, :], s, ACT.Exp, scale=SCALE).then_inc(p_hi_done, 1)
                    nc.scalar.activation(s, s, ACT.Exp, scale=SCALE).then_inc(p_done, 1)
                    if t == LAG - 1 and not first:
                        store_acc(c - 1)
                    if t == SPLIT_SLOT[0] and not first and not final:
                        split_x(j, stage0_loads(x_blocks(c)))
                    if t == SPLIT_SLOT[1] and last and not final:
                        split_x(0, stage0_loads(x_blocks(c) + 1))
                if last:
                    store_acc(c)

            act.wait_ge(weights_in, 80)
            nc.scalar.activation(wa_hi[:, :], wa_in, ACT.Copy).then_inc(w_hi_done, 1)
            nc.scalar.activation(wb_mix[:, :], wb_in, ACT.Copy).then_inc(w_hi_done, 1)
            nc.scalar.activation(wb_bias[0:R, :], wb_in[0:R, :], ACT.Copy)
            nc.scalar.activation(wb_bias[R:R + 2, :], bias_in, ACT.Copy).then_inc(w_hi_done, 1)
            nc.scalar.activation(wd_hi[:, :], wd_in, ACT.Copy).then_inc(w_hi_done, 1)
            walk(act, make, chunk)

        @block.vector
        def _(dve):
            def take_max(c, n):
                dve.wait_ge(max_made, MAXES * c + n + 1)
                kt, qb = n // QB, n % QB
                nc.vector.tensor_reduce(part_max[:, kt, qb:qb + 1], m_bank[n % 2][:, :], axis=AX.X, op=ALU.max)\
                    .then_inc(max_taken, 1)
                if n == MAXES - 1:
                    dve.wait_ge(max_taken, MAXES * (c + 1))
                    if not (isinstance(c, int) and c == 0):
                        dve.wait_ge(max_row_in, 16 * c)
                    nc.vector.tensor_reduce(neg_max[:, :], part_max[:, :, :], axis=AX.X, op=ALU.max, negate=True)\
                        .then_inc(neg_max_done, 1)

            def make(b):
                for u, (kind, i) in enumerate(KINDS):
                    if isinstance(b, int) and (kind == "q" or u == 0):
                        if u != 1:
                            dve.wait_ge(x_hi_done, i + 1)
                            at = (slice(None), 0, slice(i * CHUNK, (i + 1) * CHUNK))
                            nc.vector.tensor_tensor(x_lo[at], x_stage[:, i % STAGES, 0, :], x_hi[at], ALU.subtract)\
                                .then_inc(x_lo_done, 1)
                    dve.wait_ge(hi_done, MADE * b + u + 1)
                    src = s_bank[u % RING]
                    if kind == "v":
                        at = (slice(None), slice(i * VG, (i + 1) * VG), slice(1, L + 1))
                        nc.vector.tensor_tensor(v_lo[at], src[:, 0:VG * L].rearrange("p (t l) -> p t l", t=VG),
                                                v_hi[at], ALU.subtract).then_inc(lo_done, 1)
                    else:
                        hi, lo = (q_hi, q_lo) if kind == "q" else (k_hi, k_lo)
                        at = (slice(0, L), slice(i * CHUNK, (i + 1) * CHUNK))
                        nc.vector.tensor_tensor(lo[at], src[0:L, :], hi[at], ALU.subtract).then_inc(lo_done, 1)
                    for n in AFTER[u]:
                        take_max(b * CHUNKS, n)

            def invert(c):
                dve.wait_ge(sums_in, 16 * (c + 1))
                nc.vector.reciprocal(inverse[:, :], sums[:, :]).then_inc(inverse_done, 1)

            def add_x(c, h):
                if h == 0:
                    dve.wait_ge(x_res_in, 16 * (c + 1))
                dve.wait_ge(y_made, HALVES * c + h + 1)
                nc.vector.tensor_tensor(y_sb[:, h, :], y_bank[0:CH, :], x_res[:, h, :], ALU.add).then_inc(y_done, 1)

            def chunk(c, b, j, first=False, last=False, final=False):
                start = isinstance(c, int) and c == 0
                for t in range(QT):
                    if not last:
                        for n in MAX_IN_SLOT[t]:
                            take_max(c + 1, n)
                    dve.wait_ge(p_done, QT * c + t + 1)
                    nc.vector.tensor_tensor(p_lo[:, t % RING, :], s_bank[t % RING][:, :], p_hi[:, t % RING, :],
                                            ALU.subtract).then_inc(p_lo_done, 1)
                    if not start:
                        if t == INVERT_SLOT:
                            invert(c - 1)
                        if t in PROJECT_SLOT:
                            add_x(c - 1, PROJECT_SLOT.index(t))

            nc.vector.memset(x_lo[R:R + 2, 1, :].bitcast(F32), 1.0).then_inc(ones_set, 1)
            nc.vector.memset(q_hi[L:L + 1, :].bitcast(F32), 1.0).then_inc(ones_set, 1)
            dve.wait_ge(w_hi_done, 4)
            nc.vector.tensor_tensor(wa_lo[:, :], wa_in, wa_hi[:, :], ALU.subtract).then_inc(w_lo_done, 1)
            nc.vector.tensor_tensor(wb_mix[R:P, :], wb_in[R:P, :], wb_mix[R:P, :], ALU.subtract).then_inc(w_lo_done, 1)
            nc.vector.tensor_tensor(bias_lo[R:R + 2, :], bias_in, wb_bias[R:R + 2, :], ALU.subtract)\
                .then_inc(w_lo_done, 1)
            nc.vector.tensor_tensor(wd_lo[:, :], wd_in, wd_hi[:, :], ALU.subtract).then_inc(w_lo_done, 1)
            walk(dve, make, chunk)
            invert(B * CHUNKS - 1)
            for h in range(HALVES):
                add_x(B * CHUNKS - 1, h)


def kernel(x, L0_conv_Wt, L0_conv_bt, L0_conv_Wd, L0_conv_bd):
    import numpy as np
    import concourse.bacc as bacc
    from concourse.bass_utils import run_bass_kernel_spmd

    x = np.asarray(x)
    w, bt, wd, bd = (np.asarray(a) for a in (L0_conv_Wt, L0_conv_bt, L0_conv_Wd, L0_conv_bd))
    B, C, H, W = x.shape
    arrays = {
        "x_dram": np.ascontiguousarray(x.reshape(B, C, H * W)),
        "wt_dram": np.ascontiguousarray(w.T),
        "bt_dram": np.ascontiguousarray(bt[None]),
        "wd_dram": np.ascontiguousarray(np.concatenate([bd[None], wd.T])),
    }
    nc = bacc.Bacc("TRN2", target_bir_lowering=False, num_devices=1)
    args = [nc.dram_tensor(n, a.shape, mybir.dt.from_np(a.dtype), kind="ExternalInput").ap() for n, a in arrays.items()]
    out = nc.dram_tensor("out_dram", arrays["x_dram"].shape, mybir.dt.from_np(x.dtype), kind="ExternalOutput").ap()
    attention_conv_kernel(nc, *args, out)
    r = run_bass_kernel_spmd(nc, [arrays], core_ids=[0])
    return r.results[0]["out_dram"].reshape(B, C, H, W)
```

```python
from contextlib import ExitStack

import concourse.bass as bass
from concourse import mybir

F32 = mybir.dt.float32
F32R = mybir.dt.float32r
ALU = mybir.AluOpType
ACT = mybir.ActivationFunctionType
AX = mybir.AxisListType


def attention_conv_kernel(nc, x, wt, bt, wd, out):
    B, C, N = x.shape
    L = wd.shape[0] - 1
    W3 = 3 * L
    P = 128
    R = C - P
    HALVES = 2
    CH = C // HALVES
    CHUNK = 512
    CHUNKS = N // CHUNK
    QT = N // P
    KT = CHUNK // P
    QB = N // CHUNK
    MAXES = KT * QB
    VG = 4
    MADE = 3 * QB
    SCALE = float(L) ** -0.5
    RING = 4
    LAG = 2
    STAGES = 4
    XRING = 4
    INVERT_SLOT = 6
    PROJECT_SLOT = [16, 19]
    MAX_IN_SLOT = [[n for n in range(MAXES) if 1 + n * 26 // MAXES == t] for t in range(QT)]

    LAST_PROJECT_SLOT = [17, 19]
    LAST_MAX_IN_SLOT = [[t - 6] if t >= 6 else [] for t in range(QT)]
    TILES = [(kind, i) for i in range(QB - 1) for kind in "kqv"]
    TILES = TILES[:-1] + [("q", QB - 1), ("k", QB - 1), ("v", QB - 2), ("v", QB - 1)]
    TILE_SLOTS = {("k", 0): 3}
    for i in range(QB - 1):
        TILE_SLOTS.setdefault(("k", i), 4 * i + {4: 4, 5: 3}.get(i, 2))
        TILE_SLOTS["q", i] = 4 * i + (5 if i == 4 else 4)
        TILE_SLOTS["v", i] = 4 * i + (6 if i in (3, 4) else 5)
    del TILE_SLOTS["v", QB - 2]
    TILE_IN_SLOT = {t: TILES.index(tile) for tile, t in TILE_SLOTS.items()}
    SPLIT_IN_SLOT = {max(0, 4 * i - 2): i for i in range(QB)}
    IN_SLOTS = len(TILE_IN_SLOT)
    Q_LAST = TILES.index(("q", QB - 1))
    TILE_BANK = []
    for u in range(len(TILES)):
        TILE_BANK.append(0 if u == 0 or TILES[u] == ("v", 3) else 1 - TILE_BANK[-1])
    BEFORE_PROJECT = TILES.index(("k", 3))
    AFTER_PROJECT = TILES.index(("k", 4))

    def tile_before(u):
        return max([w + 1 for w in range(u) if TILE_BANK[w] == TILE_BANK[u]], default=0)

    def tiles_of(i):
        return max(u for u, (_, w) in enumerate(TILES) if w == i) + 1

    def last_q(n):
        return TILES.index(("q", n // KT)) + 1

    FIRST_LEFT = QT - 6
    TAIL = [("tile", IN_SLOTS), ("pv", QT - 2), ("max", FIRST_LEFT), ("max", FIRST_LEFT + 1), ("pv", QT - 1),
            ("max", MAXES - 4), ("max", MAXES - 3), ("tile", IN_SLOTS + 1), ("max", MAXES - 2), ("max", MAXES - 1),
            ("tile", IN_SLOTS + 2), ("tile", IN_SLOTS + 3)]
    START = []
    for u, (kind, i) in enumerate(TILES[:IN_SLOTS - 2]):
        START.append(("tile", u))
        if kind == "v":
            START += [("max", n) for n in range(KT * i, KT * i + KT)]
    START += [("tile", IN_SLOTS - 2), ("tile", IN_SLOTS - 1)] + [("max", n) for n in range(KT * (QB - 2), FIRST_LEFT)]
    START += [e for e in TAIL if e[0] != "pv"]

    y_view = out.rearrange("b (h c) n -> b c h n", h=HALVES)
    x_view = x.rearrange("b (h c) n -> b c h n", h=HALVES)

    ctx = ExitStack()
    with ctx:
        def sb(name, shape, dt=F32):
            return ctx.enter_context(nc.sbuf_tensor(name, shape, dt))

        def bank(name):
            return ctx.enter_context(nc.psum_tensor(name, [P, CHUNK], F32))

        def sem(name):
            return ctx.enter_context(nc.semaphore(name))

        x_stage = sb("x_stage", [P, STAGES, 2, CHUNK])
        x_hi = sb("x_hi", [P, XRING, 2, CHUNK], F32R)
        x_lo = sb("x_lo", [P, XRING, 2, CHUNK], F32R)
        wa_in = sb("wa_in", [P, W3])
        wa_hi = sb("wa_hi", [P, W3], F32R)
        wa_lo = sb("wa_lo", [P, W3], F32R)
        wb_mix = sb("wb_mix", [P, W3], F32R)
        wb_bias = sb("wb_bias", [R + 2, W3], F32R)
        bias_lo = sb("bias_lo", [R + 2, W3], F32R)
        wd_hi = sb("wd_hi", [L + 1, C], F32R)
        wd_lo = sb("wd_lo", [L + 1, C], F32R)
        q_hi = sb("q_hi", [L + 1, N], F32R)
        q_lo = sb("q_lo", [L, N], F32R)
        k_hi = sb("k_hi", [L + 1, N], F32R)
        k_lo = sb("k_lo", [L, N], F32R)
        v_hi = sb("v_hi", [P, QT, L + 2], F32R)
        v_lo = sb("v_lo", [P, QT, L + 2], F32R)
        k_max = sb("k_max", [L, KT, P], F32R)
        part_max = sb("part_max", [P, KT, QB])
        neg_max = sb("neg_max", [P, KT], F32R)
        p_hi = sb("p_hi", [P, RING, CHUNK], F32R)
        p_lo = sb("p_lo", [P, RING, CHUNK], F32R)
        acc_sb = sb("acc_sb", [L + 1, CHUNK])
        sums = sb("sums", [P, KT])
        inverse = sb("inverse", [P, KT])
        inverse_row = sb("inverse_row", [1, CHUNK])
        inverse_all = sb("inverse_all", [P, CHUNK])
        att = sb("att", [L + 1, CHUNK])
        att_hi = sb("att_hi", [L + 1, CHUNK], F32R)
        att_lo = sb("att_lo", [L + 1, CHUNK], F32R)
        x_res = sb("x_res", [CH, HALVES, CHUNK])
        y_sb = sb("y_sb", [CH, HALVES, CHUNK])
        wb_in = x_stage[:, STAGES - 2, 1, 0:W3]
        bias_in = x_stage[R:R + 2, STAGES - 1, 0, 0:W3]
        wd_in = x_stage[0:L + 1, STAGES - 1, 1, 0:C]

        s_bank = [bank(f"s_bank{i}") for i in range(RING)]
        m_bank = [bank(f"m_bank{i}") for i in range(2)]
        y_bank = bank("y_bank")
        acc_bank = bank("acc_bank")
        tile_banks = [s_bank[RING - 1], y_bank]

        def s_of(t, making):
            return s_bank[t % (RING - 1 if making else RING)][:, :]

        weights_in = sem("weights_in")
        w_hi_done = sem("w_hi_done")
        w_lo_done = sem("w_lo_done")
        bias_moved = sem("bias_moved")
        ones_set = sem("ones_set")
        x_in = [sem(f"x_in{i}") for i in range(STAGES)]
        x_hi_done = sem("x_hi_done")
        x_lo_done = sem("x_lo_done")
        made = sem("made")
        hi_done = sem("hi_done")
        lo_done = sem("lo_done")
        k_copied = sem("k_copied")
        max_made = sem("max_made")
        max_taken = sem("max_taken")
        neg_max_done = sem("neg_max_done")
        max_row_in = sem("max_row_in")
        s_made = sem("s_made")
        p_hi_done = sem("p_hi_done")
        p_done = sem("p_done")
        p_lo_done = sem("p_lo_done")
        pv_done = sem("pv_done")
        acc_out = sem("acc_out")
        sums_in = sem("sums_in")
        inverse_done = sem("inverse_done")
        inverse_row_in = sem("inverse_row_in")
        inverse_spread = sem("inverse_spread")
        att_done = sem("att_done")
        y_made = sem("y_made")
        x_res_in = sem("x_res_in")
        y_done = sem("y_done")
        y_out = sem("y_out")

        def cols(j):
            return bass.ds(j * CHUNK, CHUNK)

        def is_zero(v):
            return isinstance(v, int) and v == 0

        def walk(eng, start, chunk):
            start()
            chunk(0, 0, 0, first=True)
            with eng.Fori(0, B - 1) as b:
                c = b * CHUNKS
                with eng.Fori(1, CHUNKS - 1) as j:
                    chunk(c + j, b, j)
                chunk(c + CHUNKS - 1, b, CHUNKS - 1, making=True)
                chunk(c + CHUNKS, b + 1, 0, first=True)
            c = (B - 1) * CHUNKS
            with eng.Fori(1, CHUNKS - 1) as j:
                chunk(c + j, B - 1, j)
            chunk(c + CHUNKS - 1, B - 1, CHUNKS - 1, final=True)

        def load_x(eng, b, j):
            stage = j % STAGES
            for dst, c0, c1, part in ((slice(0, R), P, C, 1), (slice(R, P), P, C, 1), (slice(0, P), 0, P, 0)):
                eng.dma_start(x_stage[dst, stage, part, :], x[b, c0:c1, cols(j)]).then_inc(x_in[stage], 16)

        block = ctx.enter_context(nc.Block())

        @block.sync
        def _(sp):
            def y_stored(c):
                sp.wait_ge(y_out, 16 * (c + 1))

            def move_max_row(c, j, stored=None):
                sp.wait_ge(neg_max_done, c + 1)
                if stored is not None:
                    y_stored(stored)
                row = k_hi[L:L + 1, cols(j)].rearrange("o (p t) -> o p t", t=KT)
                sp.dma_start(row.bitcast(F32), neg_max[:, :].bitcast(F32)).then_inc(max_row_in, 16)

            def finish(c, b, j):
                sp.dma_start(x_res[:, :, :], x_view[b, :, :, cols(j)]).then_inc(x_res_in, 16)
                sp.wait_ge(acc_out, c + 1)
                sp.dma_start(sums[:, :], acc_sb[0:1, :].rearrange("o (p t) -> o p t", t=KT)).then_inc(sums_in, 16)
                sp.wait_ge(inverse_done, c + 1)
                sp.dma_start(inverse_row[0:1, :].rearrange("o (p t) -> o p t", t=KT), inverse[:, :])\
                    .then_inc(inverse_row_in, 16)
                sp.wait_ge(inverse_row_in, 16 * (c + 1))
                sp.dma_start(inverse_all[:, :], inverse_row[0:1, None, :].to_broadcast([1, P, CHUNK]))\
                    .then_inc(inverse_spread, 16)
                sp.wait_ge(y_done, HALVES * (c + 1))
                sp.dma_start(y_view[b, :, :, cols(j)], y_sb[:, :, :]).then_inc(y_out, 16)

            def start():
                move_max_row(0, 0)

            def chunk(c, b, j, first=False, making=False, final=False):
                if making:
                    sp.wait_ge(made, MADE * (b + 1))
                    for i in range(2):
                        load_x(sp, b + 1, i)
                if not first:
                    finish(c - 1, b, j - 1)
                elif not is_zero(c):
                    finish(c - 1, b - 1, CHUNKS - 1)
                if final:
                    y_stored(c - 1)
                else:
                    move_max_row(c + 1, 0 if making else j + 1, None if is_zero(c) else c - 1)

            for src, dst in ((wt[0:P, :], wa_in[:, :]), (wt[P:C, :], wb_in[0:R, :]), (wt[P:C, :], wb_in[R:P, :]),
                             (bt.to_broadcast([2, W3]), bias_in), (wd, wd_in)):
                sp.dma_start(dst, src).then_inc(weights_in, 16)
            for j in range(2):
                load_x(sp, 0, j)
            sp.wait_ge(w_lo_done, 4)
            sp.dma_start(wb_bias[R + 1:R + 2, :].bitcast(F32), bias_lo[R:R + 1, :].bitcast(F32)).then_inc(bias_moved, 16)
            walk(sp, start, chunk)
            finish(B * CHUNKS - 1, B - 1, CHUNKS - 1)
            y_stored(B * CHUNKS - 1)

        @block.gpsimd
        def _(pool):
            def split_x(b, j):
                pool.wait_ge(x_hi_done, QB * b + j + 1)
                for part, rows in ((0, P), (1, R)):
                    nc.gpsimd.tensor_tensor(x_lo[0:rows, j % XRING, part, :], x_stage[0:rows, j % STAGES, part, :],
                                            x_hi[0:rows, j % XRING, part, :], ALU.subtract).then_inc(x_lo_done, 1)

            def finish(c):
                pool.wait_ge(inverse_spread, 16 * (c + 1))
                for dst in (att, att_hi):
                    nc.gpsimd.tensor_tensor(dst[:, :], acc_sb[:, :], inverse_all[0:L + 1, :], ALU.mult)\
                        .then_inc(att_done, 1)
                pool.wait_ge(att_done, 3 * c + 2)
                nc.gpsimd.tensor_tensor(att_lo[:, :], att[:, :], att_hi[:, :], ALU.subtract).then_inc(att_done, 1)

            def start():
                for j in range(QB):
                    split_x(0, j)

            def chunk(c, b, j, first=False, making=False, final=False):
                if making:
                    for i in range(3):
                        split_x(b + 1, i)
                if not is_zero(c):
                    finish(c - 1)
                if making:
                    for i in range(3, QB):
                        split_x(b + 1, i)

            nc.gpsimd.memset(v_hi[:, :, 0:1].bitcast(F32), 1.0).then_inc(ones_set, 1)
            nc.gpsimd.memset(v_lo[:, :, 0:1].bitcast(F32), 0.0).then_inc(ones_set, 1)
            walk(pool, start, chunk)
            finish(B * CHUNKS - 1)

        @block.tensor
        def _(pe):
            def max_product(c, n):
                if n == 0:
                    pe.wait_ge(k_copied, c + 1)
                if n >= 2:
                    pe.wait_ge(max_taken, MAXES * c + n - 1)
                kt, qb = n % KT, n // KT
                nc.tensor.matmul(m_bank[n % 2][:, :], k_max[:, kt, :], q_hi[0:L, qb * CHUNK:(qb + 1) * CHUNK],
                                 start=True, stop=True).then_inc(max_made, 1)

            def max_product_made(b, n):
                if n % KT == 0:
                    pe.wait_ge(hi_done, MADE * b + last_q(n))
                max_product(CHUNKS * b, n)

            def make_tile(b, u, c=None):
                kind, i = TILES[u]
                if tile_before(u):
                    pe.wait_ge(lo_done, MADE * b + tile_before(u))
                if u == AFTER_PROJECT and c is not None:
                    pe.wait_ge(y_done, HALVES * c)
                pe.wait_ge(x_lo_done, 2 * (QB * b + i + 1))
                r = i % XRING
                dst = tile_banks[TILE_BANK[u]]
                if kind == "v":
                    s = slice(L, 2 * L)
                    for t in range(VG):
                        q = slice(t * P, (t + 1) * P)
                        o = dst[:, t * L:(t + 1) * L]
                        nc.tensor.matmul(o, x_stage[:, i % STAGES, 0, q], wa_in[:, s], start=True, stop=False)
                        nc.tensor.matmul(o, x_hi[:, r, 1, q], wb_mix[:, s], start=False, stop=False)
                        last = nc.tensor.matmul(o, x_lo[0:R + 2, r, 1, q], wb_bias[:, s], start=False, stop=True)
                else:
                    s = slice(0, L) if kind == "q" else slice(2 * L, 3 * L)
                    o = dst[0:L, :]
                    nc.tensor.matmul(o, wa_hi[:, s], x_hi[:, r, 0, :], start=True, stop=False)
                    nc.tensor.matmul(o, wa_lo[:, s], x_hi[:, r, 0, :], start=False, stop=False)
                    nc.tensor.matmul(o, wa_hi[:, s], x_lo[:, r, 0, :], start=False, stop=False)
                    nc.tensor.matmul(o, wb_mix[:, s], x_hi[:, r, 1, :], start=False, stop=False)
                    last = nc.tensor.matmul(o, wb_bias[:, s], x_lo[0:R + 2, r, 1, :], start=False, stop=True)
                last.then_inc(made, 1)

            def start():
                for what, n in START:
                    if what == "tile":
                        make_tile(0, n)
                    else:
                        max_product_made(0, n)

            def add_pv(c, t):
                pe.wait_ge(p_lo_done, QT * c + t + 1)
                for i, (v, p) in enumerate(((v_hi, p_hi), (v_lo, p_hi), (v_hi, p_lo))):
                    last = nc.tensor.matmul(acc_bank[0:L + 1, :], v[:, t, 0:L + 1], p[:, t % RING, :],
                                            start=(t == 0 and i == 0), stop=(t == QT - 1 and i == 2))
                last.then_inc(pv_done, 1)

            def project(c, h):
                if h == 0:
                    pe.wait_ge(att_done, 3 * (c + 1))
                else:
                    pe.wait_ge(y_done, HALVES * c + h)
                s = slice(h * CH, (h + 1) * CH)
                nc.tensor.matmul(y_bank[0:CH, :], wd_hi[:, s], att_hi[:, :], start=True, stop=False)
                nc.tensor.matmul(y_bank[0:CH, :], wd_lo[:, s], att_hi[:, :], start=False, stop=False)
                nc.tensor.matmul(y_bank[0:CH, :], wd_hi[:, s], att_lo[:, :], start=False, stop=True)\
                    .then_inc(y_made, 1)

            def chunk(c, b, j, first=False, making=False, final=False):
                pe.wait_ge(max_row_in, 16 * (c + 1))
                if first:
                    pe.wait_ge(lo_done, MADE * b + Q_LAST + 1)
                projects = LAST_PROJECT_SLOT if making else PROJECT_SLOT
                for t in range(QT):
                    if first and t == RING - 1:
                        pe.wait_ge(lo_done, MADE * (b + 1))
                    q = slice(t * P, (t + 1) * P)
                    dst = s_of(t, making)
                    nc.tensor.matmul(dst, q_hi[:, q], k_hi[:, cols(j)], start=True, stop=False)
                    nc.tensor.matmul(dst, q_hi[0:L, q], k_lo[:, cols(j)], start=False, stop=False)
                    nc.tensor.matmul(dst, q_lo[:, q], k_hi[0:L, cols(j)], start=False, stop=True).then_inc(s_made, 1)
                    if not making and not final:
                        for n in MAX_IN_SLOT[t]:
                            max_product(c + 1, n)
                    if t in projects and not is_zero(c):
                        if making and t == projects[0]:
                            pe.wait_ge(lo_done, MADE * (b + 1) + BEFORE_PROJECT + 1)
                        project(c - 1, projects.index(t))
                    if t == LAG and not is_zero(c):
                        pe.wait_ge(acc_out, c)
                    if t >= LAG:
                        add_pv(c, t - LAG)
                    elif t == 0 and not first:
                        for w in range(QT - LAG, QT):
                            add_pv(c - 1, w)
                    if making:
                        for n in LAST_MAX_IN_SLOT[t]:
                            max_product_made(b + 1, n)
                        if t in TILE_IN_SLOT:
                            make_tile(b + 1, TILE_IN_SLOT[t], c)
                if making:
                    for what, n in TAIL:
                        if what == "tile":
                            make_tile(b + 1, n)
                        elif what == "pv":
                            add_pv(c, n)
                        else:
                            max_product_made(b + 1, n)
                elif final:
                    for t in range(QT - LAG, QT):
                        add_pv(c, t)

            pe.wait_ge(w_lo_done, 4)
            pe.wait_ge(w_hi_done, 4)
            pe.wait_ge(bias_moved, 16)
            pe.wait_ge(ones_set, 4)
            walk(pe, start, chunk)
            for h in range(HALVES):
                project(B * CHUNKS - 1, h)

        @block.scalar
        def _(act):
            def split_x(b, j):
                if j >= XRING:
                    act.wait_ge(made, MADE * b + tiles_of(j - XRING))
                if 1 <= j < QB - 1:
                    if j + 1 >= STAGES:
                        act.wait_ge(made, MADE * b + tiles_of(j + 1 - STAGES))
                        act.wait_ge(x_lo_done, 2 * (QB * b + j + 2 - STAGES))
                    elif is_zero(b):
                        act.wait_ge(w_lo_done, 4)
                    load_x(act, b, j + 1)
                act.wait_ge(x_in[j % STAGES], 48 * (QB // STAGES * b + j // STAGES + 1))
                nc.scalar.activation(x_hi[:, j % XRING, :, :], x_stage[:, j % STAGES, :, :], ACT.Copy)\
                    .then_inc(x_hi_done, 1)

            def copy_k(c, j):
                src = k_hi[0:L, cols(j)].rearrange("l (p t) -> l t p", t=KT)
                nc.scalar.activation(k_max[:, :, :], src, ACT.Copy).then_inc(k_copied, 1)

            def store_acc(c):
                act.wait_ge(pv_done, QT * (c + 1))
                nc.scalar.activation(acc_sb[:, :], acc_bank[0:L + 1, :], ACT.Copy).then_inc(acc_out, 1)

            def tile_hi(b, u):
                kind, i = TILES[u]
                act.wait_ge(made, MADE * b + u + 1)
                src = tile_banks[TILE_BANK[u]]
                if kind == "v":
                    nc.scalar.activation(v_hi[:, i * VG:(i + 1) * VG, 1:L + 1],
                                         src[:, 0:VG * L].rearrange("p (t l) -> p t l", t=VG), ACT.Copy)\
                        .then_inc(hi_done, 1)
                else:
                    dst = q_hi if kind == "q" else k_hi
                    nc.scalar.activation(dst[0:L, i * CHUNK:(i + 1) * CHUNK], src[0:L, :], ACT.Copy)\
                        .then_inc(hi_done, 1)
                if u == 0:
                    act.wait_ge(hi_done, MADE * b + 1)
                    copy_k(b * CHUNKS, 0)

            def start():
                split_x(0, 0)
                for u, (kind, i) in enumerate(TILES):
                    if kind == "k" and i < QB - 1:
                        split_x(0, i + 1)
                    tile_hi(0, u)

            def chunk(c, b, j, first=False, making=False, final=False):
                if not making and not final:
                    act.wait_ge(hi_done, MADE * (b + 1))
                    act.wait_ge(max_made, MAXES * (c + 1))
                    copy_k(c + 1, j + 1)
                for t in range(QT):
                    s = s_of(t, making)
                    act.wait_ge(s_made, QT * c + t + 1)
                    if t >= RING or not first:
                        act.wait_ge(pv_done, QT * c + t - RING + 1)
                    nc.scalar.activation(p_hi[:, t % RING, :], s, ACT.Exp, scale=SCALE).then_inc(p_hi_done, 1)
                    nc.scalar.activation(s, s, ACT.Exp, scale=SCALE).then_inc(p_done, 1)
                    if t == 0 and not first:
                        store_acc(c - 1)
                    if making:
                        if t in SPLIT_IN_SLOT:
                            split_x(b + 1, SPLIT_IN_SLOT[t])
                        if t in TILE_IN_SLOT:
                            tile_hi(b + 1, TILE_IN_SLOT[t])
                if making:
                    for what, n in TAIL:
                        if what == "tile":
                            tile_hi(b + 1, n)
                        elif what == "pv" and n == QT - 1:
                            store_acc(c)
                elif final:
                    store_acc(c)

            act.wait_ge(weights_in, 80)
            nc.scalar.activation(wa_hi[:, :], wa_in[:, :], ACT.Copy).then_inc(w_hi_done, 1)
            nc.scalar.activation(wb_mix[:, :], wb_in, ACT.Copy).then_inc(w_hi_done, 1)
            nc.scalar.activation(wb_bias[0:R, :], wb_in[0:R, :], ACT.Copy)
            nc.scalar.activation(wb_bias[R:R + 2, :], bias_in, ACT.Copy).then_inc(w_hi_done, 1)
            nc.scalar.activation(wd_hi[:, :], wd_in, ACT.Copy).then_inc(w_hi_done, 1)
            walk(act, start, chunk)

        @block.vector
        def _(dve):
            def take_max(c, n):
                dve.wait_ge(max_made, MAXES * c + n + 1)
                kt, qb = n % KT, n // KT
                nc.vector.tensor_reduce(part_max[:, kt, qb:qb + 1], m_bank[n % 2][:, :], axis=AX.X, op=ALU.max)\
                    .then_inc(max_taken, 1)
                if n == MAXES - 1:
                    dve.wait_ge(max_taken, MAXES * (c + 1))
                    if not is_zero(c):
                        dve.wait_ge(max_row_in, 16 * c)
                    nc.vector.tensor_reduce(neg_max[:, :], part_max[:, :, :], axis=AX.X, op=ALU.max, negate=True)\
                        .then_inc(neg_max_done, 1)

            def tile_lo(b, u):
                kind, i = TILES[u]
                dve.wait_ge(hi_done, MADE * b + u + 1)
                src = tile_banks[TILE_BANK[u]]
                if kind == "v":
                    at = (slice(None), slice(i * VG, (i + 1) * VG), slice(1, L + 1))
                    nc.vector.tensor_tensor(v_lo[at], src[:, 0:VG * L].rearrange("p (t l) -> p t l", t=VG),
                                            v_hi[at], ALU.subtract).then_inc(lo_done, 1)
                else:
                    hi, lo = (q_hi, q_lo) if kind == "q" else (k_hi, k_lo)
                    at = (slice(0, L), slice(i * CHUNK, (i + 1) * CHUNK))
                    nc.vector.tensor_tensor(lo[at], src[0:L, :], hi[at], ALU.subtract).then_inc(lo_done, 1)

            def start():
                for what, n in START:
                    if what == "tile":
                        tile_lo(0, n)
                    elif what == "max":
                        take_max(0, n)

            def invert(c):
                dve.wait_ge(sums_in, 16 * (c + 1))
                nc.vector.reciprocal(inverse[:, :], sums[:, :]).then_inc(inverse_done, 1)

            def add_x(c, h):
                if h == 0:
                    dve.wait_ge(x_res_in, 16 * (c + 1))
                dve.wait_ge(y_made, HALVES * c + h + 1)
                nc.vector.tensor_tensor(y_sb[:, h, :], y_bank[0:CH, :], x_res[:, h, :], ALU.add).then_inc(y_done, 1)

            def chunk(c, b, j, first=False, making=False, final=False):
                projects = LAST_PROJECT_SLOT if making else PROJECT_SLOT
                for t in range(QT):
                    if making:
                        for n in LAST_MAX_IN_SLOT[t]:
                            take_max(c + 1, n)
                    elif not final:
                        for n in MAX_IN_SLOT[t]:
                            take_max(c + 1, n)
                    dve.wait_ge(p_done, QT * c + t + 1)
                    nc.vector.tensor_tensor(p_lo[:, t % RING, :], s_of(t, making), p_hi[:, t % RING, :],
                                            ALU.subtract).then_inc(p_lo_done, 1)
                    if not is_zero(c):
                        if t == INVERT_SLOT:
                            invert(c - 1)
                        if t in projects:
                            add_x(c - 1, projects.index(t))
                    if making and t in TILE_IN_SLOT:
                        tile_lo(b + 1, TILE_IN_SLOT[t])
                if making:
                    tile_lo(b + 1, IN_SLOTS)
                    for n in range(FIRST_LEFT, MAXES):
                        take_max(c + 1, n)
                    for u in range(IN_SLOTS + 1, MADE):
                        tile_lo(b + 1, u)

            nc.vector.memset(x_lo[R:R + 2, :, 1, :].bitcast(F32), 1.0).then_inc(ones_set, 1)
            nc.vector.memset(q_hi[L:L + 1, :].bitcast(F32), 1.0).then_inc(ones_set, 1)
            dve.wait_ge(w_hi_done, 4)
            nc.vector.tensor_tensor(wa_lo[:, :], wa_in[:, :], wa_hi[:, :], ALU.subtract).then_inc(w_lo_done, 1)
            nc.vector.tensor_tensor(wb_mix[R:P, :], wb_in[R:P, :], wb_mix[R:P, :], ALU.subtract).then_inc(w_lo_done, 1)
            nc.vector.tensor_tensor(bias_lo[R:R + 2, :], bias_in, wb_bias[R:R + 2, :], ALU.subtract)\
                .then_inc(w_lo_done, 1)
            nc.vector.tensor_tensor(wd_lo[:, :], wd_in, wd_hi[:, :], ALU.subtract).then_inc(w_lo_done, 1)
            walk(dve, start, chunk)
            invert(B * CHUNKS - 1)
            for h in range(HALVES):
                add_x(B * CHUNKS - 1, h)


def kernel(x, L0_conv_Wt, L0_conv_bt, L0_conv_Wd, L0_conv_bd):
    import numpy as np
    import concourse.bacc as bacc
    from concourse.bass_utils import run_bass_kernel_spmd

    x = np.asarray(x)
    w, bt, wd, bd = (np.asarray(a) for a in (L0_conv_Wt, L0_conv_bt, L0_conv_Wd, L0_conv_bd))
    B, C, H, W = x.shape
    arrays = {
        "x_dram": np.ascontiguousarray(x.reshape(B, C, H * W)),
        "wt_dram": np.ascontiguousarray(w.T),
        "bt_dram": np.ascontiguousarray(bt[None]),
        "wd_dram": np.ascontiguousarray(np.concatenate([bd[None], wd.T])),
    }
    nc = bacc.Bacc("TRN2", target_bir_lowering=False, num_devices=1)
    args = [nc.dram_tensor(n, a.shape, mybir.dt.from_np(a.dtype), kind="ExternalInput").ap() for n, a in arrays.items()]
    out = nc.dram_tensor("out_dram", arrays["x_dram"].shape, mybir.dt.from_np(x.dtype), kind="ExternalOutput").ap()
    attention_conv_kernel(nc, *args, out)
    r = run_bass_kernel_spmd(nc, [arrays], core_ids=[0])
    return r.results[0]["out_dram"].reshape(B, C, H, W)
```

```python
from contextlib import ExitStack

import concourse.bass as bass
from concourse import mybir

F32 = mybir.dt.float32
F32R = mybir.dt.float32r
ALU = mybir.AluOpType
ACT = mybir.ActivationFunctionType
AX = mybir.AxisListType


def attention_conv_kernel(nc, x, wt, bt, wd, out):
    B, C, N = x.shape
    L = wd.shape[0] - 1
    W3 = 3 * L
    P = 128
    R = C - P
    BIAS_LO = R + 32
    RB = BIAS_LO + 1
    HALVES = 2
    CH = C // HALVES
    CHUNK = 512
    CHUNKS = N // CHUNK
    QT = N // P
    KT = CHUNK // P
    QB = N // CHUNK
    MAXES = KT * QB
    VG = 4
    MADE = 3 * QB
    SCALE = float(L) ** -0.5
    RING = 4
    LAG = 2
    STAGES = 4
    XRING = 4
    INVERT_SLOT = 6
    PROJECT_SLOT = [16, 19]
    MAX_IN_SLOT = [[n for n in range(MAXES) if 1 + n * 26 // MAXES == t] for t in range(QT)]
    FIRST_MAX_IN_SLOT = [[n for n in range(MAXES) if (1 if n < 2 else 3 + (n - 2) * 25 // (MAXES - 2)) == t]
                         for t in range(QT)]

    LAST_PROJECT_SLOT = [16, 18]
    LAST_MAX_IN_SLOT = [[t - 6] if t >= 6 else [] for t in range(QT)]
    TILES = [(kind, i) for i in range(QB - 1) for kind in "kqv"]
    TILES = TILES[:-1] + [("q", QB - 1), ("k", QB - 1), ("v", QB - 2), ("v", QB - 1)]
    TILE_SLOTS = {("k", 0): 3}
    for i in range(QB - 1):
        TILE_SLOTS.setdefault(("k", i), 4 * i + {4: 4, 5: 3}.get(i, 2))
        TILE_SLOTS["q", i] = 4 * i + (5 if i == 4 else 4)
        TILE_SLOTS["v", i] = 4 * i + (6 if i in (3, 4) else 5)
    del TILE_SLOTS["v", QB - 2]
    TILE_IN_SLOT = {t: TILES.index(tile) for tile, t in TILE_SLOTS.items()}
    SPLIT_IN_SLOT = {max(0, 4 * i - 2) + part: (i, part) for i in range(QB) for part in range(2)}
    IN_SLOTS = len(TILE_IN_SLOT)
    Q_LAST = TILES.index(("q", QB - 1))
    TILE_BANK = []
    for u in range(len(TILES)):
        TILE_BANK.append(0 if u == 0 or TILES[u] == ("v", 3) else 1 - TILE_BANK[-1])
    START_BANK = [u % 4 for u in range(len(TILES) - 3)] + [1, 0, 1]
    BEFORE_PROJECT = TILES.index(("k", 3))
    AFTER_PROJECT = TILES.index(("k", 4))

    def banks_of(b):
        return START_BANK if isinstance(b, int) else TILE_BANK

    def tile_before(banks, u):
        return max([w + 1 for w in range(u) if banks[w] == banks[u]], default=0)

    def tiles_of(i):
        return max(u for u, (_, w) in enumerate(TILES) if w == i) + 1

    def last_q(n):
        return TILES.index(("q", n // KT)) + 1

    FIRST_LEFT = QT - 6
    TAIL = [("tile", IN_SLOTS), ("max", FIRST_LEFT), ("max", FIRST_LEFT + 1), ("pv", QT - 2), ("max", MAXES - 4),
            ("tile", IN_SLOTS + 1), ("max", MAXES - 3), ("pv", QT - 1), ("max", MAXES - 2), ("max", MAXES - 1),
            ("tile", IN_SLOTS + 2), ("tile", IN_SLOTS + 3)]
    START = []
    for u, (kind, i) in enumerate(TILES[:IN_SLOTS]):
        START.append(("tile", u))
        if u > 1 and kind != "q":
            START += [("max", n) for n in (range(KT * i, KT * i + 2) if kind == "v" else range(KT * i - 2, KT * i))]
    START += [("max", n) for n in range(KT * (QB - 2), FIRST_LEFT)]
    START += [e for e in TAIL if e[0] != "pv"]
    START_DVE = []
    for e in START:
        if e[0] == "max" and START_DVE and START_DVE[-1][0] == "tile":
            held = START_DVE.pop()
            START_DVE += [e, held]
        elif e[0] == "max" and len(START_DVE) > 1 and START_DVE[-2][0] == "max":
            START_DVE.insert(-1, e)
        else:
            START_DVE.append(e)

    y_view = out.rearrange("b (h c) n -> b c h n", h=HALVES)
    x_view = x.rearrange("b (h c) n -> b c h n", h=HALVES)

    ctx = ExitStack()
    with ctx:
        def sb(name, shape, dt=F32):
            return ctx.enter_context(nc.sbuf_tensor(name, shape, dt))

        def bank(name):
            return ctx.enter_context(nc.psum_tensor(name, [P, CHUNK], F32))

        def sem(name):
            return ctx.enter_context(nc.semaphore(name))

        x_stage = sb("x_stage", [P, STAGES, 2, CHUNK])
        x_hi = sb("x_hi", [P, XRING, 2, CHUNK], F32R)
        x_lo = sb("x_lo", [P, XRING, 2, CHUNK], F32R)
        wa_in = sb("wa_in", [P, W3])
        wa_hi = sb("wa_hi", [P, W3], F32R)
        wa_lo = sb("wa_lo", [P, W3], F32R)
        wb_mix = sb("wb_mix", [P, W3], F32R)
        wb_bias = sb("wb_bias", [RB, W3], F32R)
        wd_hi = sb("wd_hi", [L + 1, C], F32R)
        wd_lo = sb("wd_lo", [L + 1, C], F32R)
        q_hi = sb("q_hi", [L + 1, N], F32R)
        q_lo = sb("q_lo", [L, N], F32R)
        k_hi = sb("k_hi", [L + 1, N], F32R)
        k_lo = sb("k_lo", [L, N], F32R)
        v_hi = sb("v_hi", [P, QT, L + 2], F32R)
        v_lo = sb("v_lo", [P, QT, L + 2], F32R)
        k_max = sb("k_max", [L, KT, P], F32R)
        part_max = sb("part_max", [P, KT, QB])
        neg_max = sb("neg_max", [P, KT], F32R)
        p_hi = sb("p_hi", [P, RING, CHUNK], F32R)
        p_lo = sb("p_lo", [P, RING, CHUNK], F32R)
        acc_sb = sb("acc_sb", [L + 1, CHUNK])
        sums = sb("sums", [P, KT])
        inverse = sb("inverse", [P, KT])
        inverse_row = sb("inverse_row", [1, CHUNK])
        inverse_all = sb("inverse_all", [P, CHUNK])
        att = sb("att", [L + 1, CHUNK])
        att_hi = sb("att_hi", [L + 1, CHUNK], F32R)
        att_lo = sb("att_lo", [L + 1, CHUNK], F32R)
        x_res = sb("x_res", [CH, HALVES, CHUNK])
        y_sb = sb("y_sb", [CH, HALVES, CHUNK])
        wb_in = x_stage[:, STAGES - 2, 1, 0:W3]
        bias_in = x_stage[:, STAGES - 1, 0, 0:W3]
        wd_in = x_stage[0:L + 1, STAGES - 1, 1, 0:C]

        s_bank = [bank(f"s_bank{i}") for i in range(RING)]
        m_bank = [bank(f"m_bank{i}") for i in range(2)]
        y_bank = bank("y_bank")
        acc_bank = bank("acc_bank")
        tile_banks = [s_bank[RING - 1], y_bank, s_bank[0], s_bank[1]]

        def s_of(t, making):
            return s_bank[t % (RING - 1 if making else RING)][:, :]

        weights_in = sem("weights_in")
        bias_zeros_set = sem("bias_zeros_set")
        w_hi_done = sem("w_hi_done")
        w_lo_done = sem("w_lo_done")
        columns_set = sem("columns_set")
        q_ones_set = sem("q_ones_set")
        x_ones_set = sem("x_ones_set")
        x_in = [sem(f"x_in{i}") for i in range(STAGES)]
        x_hi_done = sem("x_hi_done")
        x_lo_done = sem("x_lo_done")
        made = sem("made")
        hi_done = sem("hi_done")
        lo_done = sem("lo_done")
        k_copied = sem("k_copied")
        max_made = sem("max_made")
        max_taken = sem("max_taken")
        neg_max_done = sem("neg_max_done")
        max_row_in = sem("max_row_in")
        s_made = sem("s_made")
        p_hi_done = sem("p_hi_done")
        p_done = sem("p_done")
        p_lo_done = sem("p_lo_done")
        pv_done = sem("pv_done")
        acc_out = sem("acc_out")
        sums_in = sem("sums_in")
        inverse_done = sem("inverse_done")
        inverse_row_in = sem("inverse_row_in")
        inverse_spread = sem("inverse_spread")
        att_done = sem("att_done")
        y_made = sem("y_made")
        x_res_in = sem("x_res_in")
        y_done = sem("y_done")
        y_out = sem("y_out")

        def cols(j):
            return bass.ds(j * CHUNK, CHUNK)

        def is_zero(v):
            return isinstance(v, int) and v == 0

        def walk(eng, start, chunk):
            start()
            chunk(0, 0, 0, first=True)
            with eng.Fori(0, B - 1) as b:
                c = b * CHUNKS
                with eng.Fori(1, CHUNKS - 1) as j:
                    chunk(c + j, b, j)
                chunk(c + CHUNKS - 1, b, CHUNKS - 1, making=True)
                chunk(c + CHUNKS, b + 1, 0, first=True)
            c = (B - 1) * CHUNKS
            with eng.Fori(1, CHUNKS - 1) as j:
                chunk(c + j, B - 1, j)
            chunk(c + CHUNKS - 1, B - 1, CHUNKS - 1, final=True)

        def load_x(eng, b, j):
            stage = j % STAGES
            for dst, c0, c1, part in ((slice(0, R), P, C, 1), (slice(R, P), P, C, 1), (slice(0, P), 0, P, 0)):
                eng.dma_start(x_stage[dst, stage, part, :], x[b, c0:c1, cols(j)]).then_inc(x_in[stage], 16)

        block = ctx.enter_context(nc.Block())

        @block.sync
        def _(sp):
            def y_stored(c):
                sp.wait_ge(y_out, 16 * (c + 1))

            def move_max_row(c, j, stored=None):
                sp.wait_ge(neg_max_done, c + 1)
                if stored is not None:
                    y_stored(stored)
                row = k_hi[L:L + 1, cols(j)].rearrange("o (p t) -> o p t", t=KT)
                sp.dma_start(row.bitcast(F32), neg_max[:, :].bitcast(F32)).then_inc(max_row_in, 16)

            def finish(c, b, j):
                sp.dma_start(x_res[:, :, :], x_view[b, :, :, cols(j)]).then_inc(x_res_in, 16)
                sp.wait_ge(acc_out, c + 1)
                sp.dma_start(sums[:, :], acc_sb[0:1, :].rearrange("o (p t) -> o p t", t=KT)).then_inc(sums_in, 16)
                sp.wait_ge(inverse_done, c + 1)
                sp.dma_start(inverse_row[0:1, :].rearrange("o (p t) -> o p t", t=KT), inverse[:, :])\
                    .then_inc(inverse_row_in, 16)
                sp.wait_ge(inverse_row_in, 16 * (c + 1))
                sp.dma_start(inverse_all[:, :], inverse_row[0:1, None, :].to_broadcast([1, P, CHUNK]))\
                    .then_inc(inverse_spread, 16)
                sp.wait_ge(y_done, HALVES * (c + 1))
                sp.dma_start(y_view[b, :, :, cols(j)], y_sb[:, :, :]).then_inc(y_out, 16)

            def start():
                move_max_row(0, 0)

            def chunk(c, b, j, first=False, making=False, final=False):
                if making:
                    sp.wait_ge(made, MADE * (b + 1))
                    for i in range(2):
                        load_x(sp, b + 1, i)
                if not first:
                    finish(c - 1, b, j - 1)
                elif not is_zero(c):
                    finish(c - 1, b - 1, CHUNKS - 1)
                if final:
                    y_stored(c - 1)
                else:
                    move_max_row(c + 1, 0 if making else j + 1, None if is_zero(c) else c - 1)

            for src, dst in ((wt[0:P, :], wa_in[:, :]), (bt.to_broadcast([RB - R, W3]), bias_in[R:RB, :]),
                             (wt[P:C, :], wb_in[0:R, :]), (wt[P:C, :], wb_in[R:P, :]), (wd, wd_in)):
                sp.dma_start(dst, src).then_inc(weights_in, 16)
            for j in range(2):
                load_x(sp, 0, j)
            walk(sp, start, chunk)
            finish(B * CHUNKS - 1, B - 1, CHUNKS - 1)
            y_stored(B * CHUNKS - 1)

        @block.gpsimd
        def _(pool):
            def split_x(b, j):
                for part, rows in ((0, P), (1, R)):
                    pool.wait_ge(x_hi_done, 2 * (QB * b + j) + part + 1)
                    nc.gpsimd.tensor_tensor(x_lo[0:rows, j % XRING, part, :], x_stage[0:rows, j % STAGES, part, :],
                                            x_hi[0:rows, j % XRING, part, :], ALU.subtract).then_inc(x_lo_done, 1)

            def finish(c):
                pool.wait_ge(inverse_spread, 16 * (c + 1))
                for dst in (att, att_hi):
                    nc.gpsimd.tensor_tensor(dst[:, :], acc_sb[:, :], inverse_all[0:L + 1, :], ALU.mult)\
                        .then_inc(att_done, 1)
                pool.wait_ge(att_done, 3 * c + 2)
                nc.gpsimd.tensor_tensor(att_lo[:, :], att[:, :], att_hi[:, :], ALU.subtract).then_inc(att_done, 1)

            def start():
                for j in range(QB):
                    split_x(0, j)

            def chunk(c, b, j, first=False, making=False, final=False):
                if making:
                    for i in range(3):
                        split_x(b + 1, i)
                if not is_zero(c):
                    finish(c - 1)
                if making:
                    for i in range(3, QB):
                        split_x(b + 1, i)

            nc.gpsimd.memset(v_hi[:, :, 0:1].bitcast(F32), 1.0).then_inc(columns_set, 1)
            nc.gpsimd.memset(v_lo[:, :, 0:1].bitcast(F32), 0.0).then_inc(columns_set, 1)
            pool.wait_ge(columns_set, 2)
            nc.gpsimd.memset(q_hi[L:L + 1, :].bitcast(F32), 1.0).then_inc(q_ones_set, 1)
            pool.wait_ge(q_ones_set, 1)
            walk(pool, start, chunk)

        @block.tensor
        def _(pe):
            def max_product(c, n):
                if n == 0:
                    pe.wait_ge(k_copied, c + 1)
                if n >= 2:
                    pe.wait_ge(max_taken, MAXES * c + n - 1)
                kt, qb = n % KT, n // KT
                nc.tensor.matmul(m_bank[n % 2][:, :], k_max[:, kt, :], q_hi[0:L, qb * CHUNK:(qb + 1) * CHUNK],
                                 start=True, stop=True).then_inc(max_made, 1)

            def max_product_made(b, n):
                if n % KT == 0:
                    pe.wait_ge(hi_done, MADE * b + last_q(n))
                max_product(CHUNKS * b, n)

            def make_tile(b, u, c=None):
                kind, i = TILES[u]
                before = tile_before(banks_of(b), u)
                if before:
                    pe.wait_ge(lo_done, MADE * b + before)
                if u == AFTER_PROJECT and c is not None:
                    pe.wait_ge(y_done, HALVES * c)
                pe.wait_ge(x_hi_done, 2 * (QB * b + i + 1))
                r = i % XRING
                dst = tile_banks[banks_of(b)[u]]
                if kind == "v":
                    s = slice(L, 2 * L)
                    for t in range(VG):
                        q = slice(t * P, (t + 1) * P)
                        o = dst[:, t * L:(t + 1) * L]
                        nc.tensor.matmul(o, x_stage[:, i % STAGES, 0, q], wa_in[:, s], start=True, stop=False)
                        nc.tensor.matmul(o, x_hi[:, r, 1, q], wb_mix[:, s], start=False, stop=False)
                        last = nc.tensor.matmul(o, x_lo[0:RB, r, 1, q], wb_bias[:, s], start=False, stop=True)
                else:
                    s = slice(0, L) if kind == "q" else slice(2 * L, 3 * L)
                    o = dst[0:L, :]
                    nc.tensor.matmul(o, wa_hi[:, s], x_hi[:, r, 0, :], start=True, stop=False)
                    nc.tensor.matmul(o, wa_lo[:, s], x_hi[:, r, 0, :], start=False, stop=False)
                    nc.tensor.matmul(o, wb_mix[:, s], x_hi[:, r, 1, :], start=False, stop=False)
                    pe.wait_ge(x_lo_done, 2 * (QB * b + i + 1))
                    nc.tensor.matmul(o, wa_hi[:, s], x_lo[:, r, 0, :], start=False, stop=False)
                    last = nc.tensor.matmul(o, wb_bias[:, s], x_lo[0:RB, r, 1, :], start=False, stop=True)
                last.then_inc(made, 1)

            def start():
                for what, n in START:
                    if what == "tile":
                        make_tile(0, n)
                    else:
                        max_product_made(0, n)

            def add_pv(c, t):
                pe.wait_ge(p_lo_done, QT * c + t + 1)
                for i, (v, p) in enumerate(((v_hi, p_hi), (v_lo, p_hi), (v_hi, p_lo))):
                    last = nc.tensor.matmul(acc_bank[0:L + 1, :], v[:, t, 0:L + 1], p[:, t % RING, :],
                                            start=(t == 0 and i == 0), stop=(t == QT - 1 and i == 2))
                last.then_inc(pv_done, 1)

            def project(c, h):
                if h == 0:
                    pe.wait_ge(att_done, 3 * (c + 1))
                else:
                    pe.wait_ge(y_done, HALVES * c + h)
                s = slice(h * CH, (h + 1) * CH)
                nc.tensor.matmul(y_bank[0:CH, :], wd_hi[:, s], att_hi[:, :], start=True, stop=False)
                nc.tensor.matmul(y_bank[0:CH, :], wd_lo[:, s], att_hi[:, :], start=False, stop=False)
                nc.tensor.matmul(y_bank[0:CH, :], wd_hi[:, s], att_lo[:, :], start=False, stop=True)\
                    .then_inc(y_made, 1)

            def chunk(c, b, j, first=False, making=False, final=False):
                pe.wait_ge(max_row_in, 16 * (c + 1))
                if first:
                    pe.wait_ge(lo_done, MADE * b + Q_LAST + 1)
                projects = LAST_PROJECT_SLOT if making else PROJECT_SLOT
                for t in range(QT):
                    if first and t == RING - 1:
                        pe.wait_ge(lo_done, MADE * (b + 1))
                    q = slice(t * P, (t + 1) * P)
                    dst = s_of(t, making)
                    nc.tensor.matmul(dst, q_hi[:, q], k_hi[:, cols(j)], start=True, stop=False)
                    nc.tensor.matmul(dst, q_hi[0:L, q], k_lo[:, cols(j)], start=False, stop=False)
                    nc.tensor.matmul(dst, q_lo[:, q], k_hi[0:L, cols(j)], start=False, stop=True).then_inc(s_made, 1)
                    if not making and not final:
                        for n in (FIRST_MAX_IN_SLOT if first else MAX_IN_SLOT)[t]:
                            max_product(c + 1, n)
                    if t in projects and not is_zero(c):
                        if making and t == projects[0]:
                            pe.wait_ge(lo_done, MADE * (b + 1) + BEFORE_PROJECT + 1)
                        project(c - 1, projects.index(t))
                    if t == LAG and not is_zero(c):
                        pe.wait_ge(acc_out, c)
                    if t >= LAG:
                        add_pv(c, t - LAG)
                    elif t == 0 and not first:
                        for w in range(QT - LAG, QT):
                            add_pv(c - 1, w)
                    if making:
                        for n in LAST_MAX_IN_SLOT[t]:
                            max_product_made(b + 1, n)
                        if t in TILE_IN_SLOT:
                            make_tile(b + 1, TILE_IN_SLOT[t], c)
                if making:
                    for what, n in TAIL:
                        if what == "tile":
                            make_tile(b + 1, n)
                        elif what == "pv":
                            add_pv(c, n)
                        else:
                            max_product_made(b + 1, n)
                elif final:
                    for t in range(QT - LAG, QT):
                        add_pv(c, t)

            pe.wait_ge(columns_set, 2)
            pe.wait_ge(q_ones_set, 1)
            pe.wait_ge(x_ones_set, 1)
            pe.wait_ge(w_hi_done, 4)
            pe.wait_ge(w_lo_done, 4)
            walk(pe, start, chunk)
            for h in range(HALVES):
                project(B * CHUNKS - 1, h)

        @block.scalar
        def _(act):
            def split_x(b, j, part):
                if part == 0:
                    load_next(b, j)
                nc.scalar.activation(x_hi[:, j % XRING, part, :], x_stage[:, j % STAGES, part, :], ACT.Copy)\
                    .then_inc(x_hi_done, 1)

            def load_next(b, j):
                if j >= XRING:
                    act.wait_ge(made, MADE * b + tiles_of(j - XRING))
                if 1 <= j < QB - 1:
                    if j + 1 >= STAGES:
                        act.wait_ge(made, MADE * b + tiles_of(j + 1 - STAGES))
                        act.wait_ge(x_lo_done, 2 * (QB * b + j + 2 - STAGES))
                    elif is_zero(b):
                        act.wait_ge(w_lo_done, 4)
                    load_x(act, b, j + 1)
                act.wait_ge(x_in[j % STAGES], 48 * (QB // STAGES * b + j // STAGES + 1))

            def copy_k(c, j):
                src = k_hi[0:L, cols(j)].rearrange("l (p t) -> l t p", t=KT)
                nc.scalar.activation(k_max[:, :, :], src, ACT.Copy).then_inc(k_copied, 1)

            def store_acc(c):
                act.wait_ge(pv_done, QT * (c + 1))
                nc.scalar.activation(acc_sb[:, :], acc_bank[0:L + 1, :], ACT.Copy).then_inc(acc_out, 1)

            def tile_hi(b, u):
                kind, i = TILES[u]
                act.wait_ge(made, MADE * b + u + 1)
                src = tile_banks[banks_of(b)[u]]
                if kind == "v":
                    nc.scalar.activation(v_hi[:, i * VG:(i + 1) * VG, 1:L + 1],
                                         src[:, 0:VG * L].rearrange("p (t l) -> p t l", t=VG), ACT.Copy)\
                        .then_inc(hi_done, 1)
                else:
                    dst = q_hi if kind == "q" else k_hi
                    nc.scalar.activation(dst[0:L, i * CHUNK:(i + 1) * CHUNK], src[0:L, :], ACT.Copy)\
                        .then_inc(hi_done, 1)
                if u == 0:
                    act.wait_ge(hi_done, MADE * b + 1)
                    copy_k(b * CHUNKS, 0)

            def copy_second_k(b):
                act.wait_ge(hi_done, MADE * b + TILES.index(("k", QB - 1)) + 1)
                act.wait_ge(max_made, MAXES * (CHUNKS * b + 1))
                copy_k(CHUNKS * b + 1, 1)

            def start():
                for part in range(2):
                    split_x(0, 0, part)
                for u, (kind, i) in enumerate(TILES):
                    if kind == "k" and i < QB - 1:
                        for part in range(2):
                            split_x(0, i + 1, part)
                    if u == MADE - 2:
                        copy_second_k(0)
                    tile_hi(0, u)

            def chunk(c, b, j, first=False, making=False, final=False):
                if not first and not making and not final:
                    act.wait_ge(max_made, MAXES * (c + 1))
                    copy_k(c + 1, j + 1)
                for t in range(QT):
                    s = s_of(t, making)
                    act.wait_ge(s_made, QT * c + t + 1)
                    if t >= RING or not first:
                        act.wait_ge(pv_done, QT * c + t - RING + 1)
                    nc.scalar.activation(p_hi[:, t % RING, :], s, ACT.Exp, scale=SCALE).then_inc(p_hi_done, 1)
                    nc.scalar.activation(s, s, ACT.Exp, scale=SCALE).then_inc(p_done, 1)
                    if t == 0 and not first:
                        store_acc(c - 1)
                    if making:
                        if t in SPLIT_IN_SLOT:
                            split_x(b + 1, *SPLIT_IN_SLOT[t])
                        if t in TILE_IN_SLOT:
                            tile_hi(b + 1, TILE_IN_SLOT[t])
                if making:
                    for what, n in TAIL:
                        if what == "tile":
                            if n == MADE - 2:
                                copy_second_k(b + 1)
                            tile_hi(b + 1, n)
                        elif what == "pv" and n == QT - 1:
                            store_acc(c)
                elif final:
                    store_acc(c)

            act.wait_ge(weights_in, 80)
            nc.scalar.activation(wa_hi[:, :], wa_in[:, :], ACT.Copy).then_inc(w_hi_done, 1)
            nc.scalar.activation(wb_mix[:, :], wb_in, ACT.Copy).then_inc(w_hi_done, 1)
            act.wait_ge(bias_zeros_set, 1)
            nc.scalar.activation(wb_bias[0:R, :], wb_in[0:R, :], ACT.Copy)
            nc.scalar.activation(wb_bias[R:R + 1, :], bias_in[R:R + 1, :], ACT.Copy)
            nc.scalar.activation(wb_bias[BIAS_LO:RB, :], bias_in[BIAS_LO:RB, :], ACT.Copy).then_inc(w_hi_done, 1)
            nc.scalar.activation(wd_hi[:, :], wd_in, ACT.Copy).then_inc(w_hi_done, 1)
            walk(act, start, chunk)

        @block.vector
        def _(dve):
            def take_max(c, n):
                dve.wait_ge(max_made, MAXES * c + n + 1)
                kt, qb = n % KT, n // KT
                nc.vector.tensor_reduce(part_max[:, kt, qb:qb + 1], m_bank[n % 2][:, :], axis=AX.X, op=ALU.max)\
                    .then_inc(max_taken, 1)
                if n == MAXES - 1:
                    dve.wait_ge(max_taken, MAXES * (c + 1))
                    if not is_zero(c):
                        dve.wait_ge(max_row_in, 16 * c)
                    nc.vector.tensor_reduce(neg_max[:, :], part_max[:, :, :], axis=AX.X, op=ALU.max, negate=True)\
                        .then_inc(neg_max_done, 1)

            def tile_lo(b, u):
                kind, i = TILES[u]
                dve.wait_ge(hi_done, MADE * b + u + 1)
                src = tile_banks[banks_of(b)[u]]
                if kind == "v":
                    at = (slice(None), slice(i * VG, (i + 1) * VG), slice(1, L + 1))
                    nc.vector.tensor_tensor(v_lo[at], src[:, 0:VG * L].rearrange("p (t l) -> p t l", t=VG),
                                            v_hi[at], ALU.subtract).then_inc(lo_done, 1)
                else:
                    hi, lo = (q_hi, q_lo) if kind == "q" else (k_hi, k_lo)
                    at = (slice(0, L), slice(i * CHUNK, (i + 1) * CHUNK))
                    nc.vector.tensor_tensor(lo[at], src[0:L, :], hi[at], ALU.subtract).then_inc(lo_done, 1)

            def start():
                for what, n in START_DVE:
                    if what == "tile":
                        tile_lo(0, n)
                    elif what == "max":
                        take_max(0, n)

            def invert(c):
                dve.wait_ge(sums_in, 16 * (c + 1))
                nc.vector.reciprocal(inverse[:, :], sums[:, :]).then_inc(inverse_done, 1)

            def add_x(c, h):
                if h == 0:
                    dve.wait_ge(x_res_in, 16 * (c + 1))
                dve.wait_ge(y_made, HALVES * c + h + 1)
                nc.vector.tensor_tensor(y_sb[:, h, :], y_bank[0:CH, :], x_res[:, h, :], ALU.add).then_inc(y_done, 1)

            def chunk(c, b, j, first=False, making=False, final=False):
                projects = LAST_PROJECT_SLOT if making else PROJECT_SLOT
                for t in range(QT):
                    if making:
                        for n in LAST_MAX_IN_SLOT[t]:
                            take_max(c + 1, n)
                    elif not final:
                        for n in (FIRST_MAX_IN_SLOT if first else MAX_IN_SLOT)[t]:
                            take_max(c + 1, n)
                    dve.wait_ge(p_done, QT * c + t + 1)
                    nc.vector.tensor_tensor(p_lo[:, t % RING, :], s_of(t, making), p_hi[:, t % RING, :],
                                            ALU.subtract).then_inc(p_lo_done, 1)
                    if not is_zero(c):
                        if t == INVERT_SLOT:
                            invert(c - 1)
                        if t in projects:
                            add_x(c - 1, projects.index(t))
                    if making and t in TILE_IN_SLOT:
                        tile_lo(b + 1, TILE_IN_SLOT[t])
                if making:
                    last_block = KT * (QB - 1)
                    for n in range(FIRST_LEFT, MAXES):
                        if n == last_block:
                            tile_lo(b + 1, IN_SLOTS)
                        take_max(c + 1, n)
                    for u in range(IN_SLOTS + 1, MADE):
                        tile_lo(b + 1, u)

            nc.vector.memset(wb_bias[R:BIAS_LO, :].bitcast(F32), 0.0).then_inc(bias_zeros_set, 1)
            nc.vector.memset(x_lo[R:RB, :, 1, :].bitcast(F32), 1.0).then_inc(x_ones_set, 1)
            dve.wait_ge(w_hi_done, 1)
            nc.vector.tensor_tensor(wa_lo[:, :], wa_in[:, :], wa_hi[:, :], ALU.subtract).then_inc(w_lo_done, 1)
            dve.wait_ge(w_hi_done, 2)
            nc.vector.tensor_tensor(wb_mix[R:P, :], wb_in[R:P, :], wb_mix[R:P, :], ALU.subtract).then_inc(w_lo_done, 1)
            dve.wait_ge(w_hi_done, 3)
            nc.vector.tensor_tensor(wb_bias[BIAS_LO:RB, :], bias_in[BIAS_LO:RB, :], wb_bias[BIAS_LO:RB, :],
                                    ALU.subtract).then_inc(w_lo_done, 1)
            dve.wait_ge(w_hi_done, 4)
            nc.vector.tensor_tensor(wd_lo[:, :], wd_in, wd_hi[:, :], ALU.subtract).then_inc(w_lo_done, 1)
            walk(dve, start, chunk)
            c = B * CHUNKS - 1
            invert(c)
            dve.wait_ge(inverse_spread, 16 * (c + 1))
            for dst in (att, att_hi):
                nc.vector.tensor_tensor(dst[:, :], acc_sb[:, :], inverse_all[0:L + 1, :], ALU.mult)\
                    .then_inc(att_done, 1)
            dve.wait_ge(att_done, 3 * c + 2)
            nc.vector.tensor_tensor(att_lo[:, :], att[:, :], att_hi[:, :], ALU.subtract).then_inc(att_done, 1)
            for h in range(HALVES):
                add_x(c, h)


def kernel(x, L0_conv_Wt, L0_conv_bt, L0_conv_Wd, L0_conv_bd):
    import numpy as np
    import concourse.bacc as bacc
    from concourse.bass_utils import run_bass_kernel_spmd

    x = np.asarray(x)
    w, bt, wd, bd = (np.asarray(a) for a in (L0_conv_Wt, L0_conv_bt, L0_conv_Wd, L0_conv_bd))
    B, C, H, W = x.shape
    arrays = {
        "x_dram": np.ascontiguousarray(x.reshape(B, C, H * W)),
        "wt_dram": np.ascontiguousarray(w.T),
        "bt_dram": np.ascontiguousarray(bt[None]),
        "wd_dram": np.ascontiguousarray(np.concatenate([bd[None], wd.T])),
    }
    nc = bacc.Bacc("TRN2", target_bir_lowering=False, num_devices=1)
    args = [nc.dram_tensor(n, a.shape, mybir.dt.from_np(a.dtype), kind="ExternalInput").ap() for n, a in arrays.items()]
    out = nc.dram_tensor("out_dram", arrays["x_dram"].shape, mybir.dt.from_np(x.dtype), kind="ExternalOutput").ap()
    attention_conv_kernel(nc, *args, out)
    r = run_bass_kernel_spmd(nc, [arrays], core_ids=[0])
    return r.results[0]["out_dram"].reshape(B, C, H, W)
```
